# Optimizing a Trainium2 kernel written in Bass

```python
import numpy as np
import jax
import jax.numpy as jnp

def _softmax(x, axis=-1):
    return jax.nn.softmax(x, axis=axis)

def _gelu(x):
    return jax.nn.gelu(x, approximate=True)

def _silu(x):
    return jax.nn.silu(x)

def _sigmoid(x):
    return jax.nn.sigmoid(x)

def _layernorm(x, axis=-1, eps=1e-05):
    m = jnp.mean(x, axis=axis, keepdims=True)
    v = jnp.var(x, axis=axis, keepdims=True)
    return (x - m) / jnp.sqrt(v + eps)

def _scatter_add(tgt, idx, src, axis=0):
    return tgt.at[idx].add(src)

def _segment_sum(src, seg, n):
    return jax.ops.segment_sum(src, seg, n)
kernel_name = 'mk_gnn_resnorm_d2_gnn_r8_989f23'

def setup_inputs(seed: int=0):
    np.random.seed(seed)
    _w = jnp.asarray

    def _rec_inputs():
        import jax
        import jax.numpy as jnp
        _gk = jax.random.key(seed)
        x = -0.000202 + 1 * jax.random.normal(jax.random.fold_in(_gk, 1), (12500, 64), jnp.float32)
        src = jax.random.randint(jax.random.fold_in(_gk, 2), (400000,), 0, 12500, jnp.int32)
        dst = jnp.minimum((12500 * jax.random.uniform(jax.random.fold_in(_gk, 3), (400000,)) ** 2.0).astype(jnp.int32), 99999)
        _o = jnp.argsort(dst, stable=True)
        src = src[_o]
        dst = dst[_o]
        edge_attr_64 = -8.16379e-05 + 0.999858 * jax.random.normal(jax.random.fold_in(_gk, 11), (400000, 64), jnp.float32)
        return (x, src, dst, edge_attr_64)
    x, src, dst, edge_attr_64 = _rec_inputs()

    def _L0_gnn_setup():
        import jax, jax.numpy as jnp
        import numpy as np
        N_NODES = 12500
        N_EDGES = 156250
        D_IN = 64
        D_HID = 64
        D_OUT = 64

        def sage_conv(x, src, dst, W_l, b_l, W_r, n_nodes):
            msgs = x[src]
            agg = jax.ops.segment_sum(msgs, dst, num_segments=n_nodes)
            cnt = jax.ops.segment_sum(jnp.ones((src.shape[0],), x.dtype), dst, num_segments=n_nodes)
            mean = agg / jnp.maximum(cnt, 1.0)[:, None]
            return mean @ W_l.T + b_l + x @ W_r.T
        key = jax.random.key(seed)
        k1, k2, k3, k4, k5, k6, k7 = jax.random.split(key, 7)
        x = jax.random.normal(k1, (N_NODES, D_IN), dtype=jnp.float32)
        edge_index = jax.random.randint(k2, (2, N_EDGES), 0, N_NODES, dtype=jnp.int64)
        s1 = 1.0 / np.sqrt(D_IN)
        s2 = 1.0 / np.sqrt(D_HID)
        W1_l = jax.random.uniform(k3, (D_HID, D_IN), jnp.float32, -s1, s1)
        b1_l = jnp.zeros((D_HID,), jnp.float32)
        W1_r = jax.random.uniform(k4, (D_HID, D_IN), jnp.float32, -s1, s1)
        W2_l = jax.random.uniform(k5, (D_OUT, D_HID), jnp.float32, -s2, s2)
        b2_l = jnp.zeros((D_OUT,), jnp.float32)
        W2_r = jax.random.uniform(k6, (D_OUT, D_HID), jnp.float32, -s2, s2)
        return {'x': x, 'edge_index': edge_index, 'W1_l': W1_l, 'b1_l': b1_l, 'W1_r': W1_r, 'W2_l': W2_l, 'b2_l': b2_l, 'W2_r': W2_r}
    _L0_gnn_all = _L0_gnn_setup()
    _L0_gnn_in = {k: v for k, v in _L0_gnn_all.items() if k in ('W1_l', 'b1_l', 'W1_r', 'W2_l', 'b2_l', 'W2_r')}
    del _L0_gnn_all

    def _L1_gnn_setup():
        import jax, jax.numpy as jnp
        import numpy as np
        N = 6250
        EG = 200000
        IN = 64
        OUT = 64
        H = 4
        D = OUT // H
        key = jax.random.key(seed)
        ks = jax.random.split(key, 12)
        s = 1.0 / np.sqrt(IN)
        return {'x': jax.random.normal(ks[0], (N, IN), jnp.float32), 'edge_attr': jax.random.normal(ks[1], (EG, IN), jnp.float32), 'edge_index': jax.random.randint(ks[2], (2, EG), 0, N, jnp.int32), 'Wq': jax.random.uniform(ks[3], (OUT, IN), jnp.float32, -s, s), 'bq': jax.random.uniform(ks[4], (OUT,), jnp.float32, -s, s), 'Wk': jax.random.uniform(ks[5], (OUT, IN), jnp.float32, -s, s), 'bk': jax.random.uniform(ks[6], (OUT,), jnp.float32, -s, s), 'We': jax.random.uniform(ks[7], (OUT, IN), jnp.float32, -s, s), 'be': jax.random.uniform(ks[8], (OUT,), jnp.float32, -s, s), 'Wv': jax.random.uniform(ks[9], (OUT, IN), jnp.float32, -s, s), 'bv': jax.random.uniform(ks[10], (OUT,), jnp.float32, -s, s)}
    _L1_gnn_all = _L1_gnn_setup()
    _L1_gnn_in = {k: v for k, v in _L1_gnn_all.items() if k in ('Wq', 'bq', 'Wk', 'bk', 'We', 'be', 'Wv', 'bv')}
    del _L1_gnn_all
    return {'x': x, 'src': src, 'dst': dst, 'edge_attr_64': edge_attr_64, 'L0_gnn_W1_l': _L0_gnn_in['W1_l'], 'L0_gnn_b1_l': _L0_gnn_in['b1_l'], 'L0_gnn_W1_r': _L0_gnn_in['W1_r'], 'L0_gnn_W2_l': _L0_gnn_in['W2_l'], 'L0_gnn_b2_l': _L0_gnn_in['b2_l'], 'L0_gnn_W2_r': _L0_gnn_in['W2_r'], 'L1_gnn_Wq': _L1_gnn_in['Wq'], 'L1_gnn_bq': _L1_gnn_in['bq'], 'L1_gnn_Wk': _L1_gnn_in['Wk'], 'L1_gnn_bk': _L1_gnn_in['bk'], 'L1_gnn_We': _L1_gnn_in['We'], 'L1_gnn_be': _L1_gnn_in['be'], 'L1_gnn_Wv': _L1_gnn_in['Wv'], 'L1_gnn_bv': _L1_gnn_in['bv']}

def reference(x, src, dst, edge_attr_64, L0_gnn_W1_l, L0_gnn_b1_l, L0_gnn_W1_r, L0_gnn_W2_l, L0_gnn_b2_l, L0_gnn_W2_r, L1_gnn_Wq, L1_gnn_bq, L1_gnn_Wk, L1_gnn_bk, L1_gnn_We, L1_gnn_be, L1_gnn_Wv, L1_gnn_bv):
    import jax
    import jax.numpy as jnp

    def _L0_gnn_ref(x, edge_index, W1_l, b1_l, W1_r, W2_l, b2_l, W2_r):
        import jax, jax.numpy as jnp
        import numpy as np
        N_NODES = 12500
        N_EDGES = 156250
        D_IN = 64
        D_HID = 64
        D_OUT = 64

        def sage_conv(x, src, dst, W_l, b_l, W_r, n_nodes):
            msgs = x[src]
            agg = jax.ops.segment_sum(msgs, dst, num_segments=n_nodes)
            cnt = jax.ops.segment_sum(jnp.ones((src.shape[0],), x.dtype), dst, num_segments=n_nodes)
            mean = agg / jnp.maximum(cnt, 1.0)[:, None]
            return mean @ W_l.T + b_l + x @ W_r.T
        src, dst = (edge_index[0], edge_index[1])
        n = x.shape[0]
        h = sage_conv(x, src, dst, W1_l, b1_l, W1_r, n)
        h = jax.nn.relu(h)
        out = sage_conv(h, src, dst, W2_l, b2_l, W2_r, n)
        return out

    def _L1_gnn_ref(x, edge_attr, edge_index, Wq, bq, Wk, bk, We, be, Wv, bv):
        import jax, jax.numpy as jnp
        import numpy as np
        N = 6250
        EG = 200000
        IN = 64
        OUT = 64
        H = 4
        D = OUT // H
        n = x.shape[0]
        Qh = (x @ Wq.T + bq).reshape(n, H, D)
        Kh = (x @ Wk.T + bk).reshape(n, H, D)
        Vh = (x @ Wv.T + bv).reshape(n, H, D)
        Ee = (edge_attr @ We.T + be).reshape(-1, H, D)
        src = edge_index[0]
        dst = edge_index[1]
        score = (Kh[src] * Qh[dst] * (1.0 / np.sqrt(D)) * Ee).sum(-1)
        score = jnp.exp(jnp.clip(score, -5.0, 5.0))
        msg = Vh[src] * score[..., None]
        wV = jax.ops.segment_sum(msg, dst, num_segments=n)
        return wV.reshape(n, H * D)
    edge_index = jnp.stack([src, dst])
    x = _layernorm(x + _L0_gnn_ref(x, edge_index, L0_gnn_W1_l, L0_gnn_b1_l, L0_gnn_W1_r, L0_gnn_W2_l, L0_gnn_b2_l, L0_gnn_W2_r), axis=-1)
    x = _layernorm(x + _L1_gnn_ref(x, edge_attr_64, edge_index, L1_gnn_Wq, L1_gnn_bq, L1_gnn_Wk, L1_gnn_bk, L1_gnn_We, L1_gnn_be, L1_gnn_Wv, L1_gnn_bv), axis=-1)
    return x

_drawn_inputs = setup_inputs


def setup_inputs(seed=0):
    import zlib

    import numpy as np

    out = dict(_drawn_inputs(seed))
    spreads = {'L0_gnn_b1_l': (0.0, 0.1), 'L0_gnn_b2_l': (0.0, 0.1)}
    factors = {'L1_gnn_bq': 4.152, 'L1_gnn_bk': 3.528, 'L1_gnn_be': 3.456}
    for name, (base, spread) in spreads.items():
        noise = np.random.default_rng([zlib.crc32(name.encode()), seed]).standard_normal(out[name].shape)
        drawn = base * np.exp(spread * noise) if base else spread * noise
        out[name] = jnp.asarray(drawn.astype(out[name].dtype))
    for name, factor in factors.items():
        out[name] = (out[name] * factor).astype(out[name].dtype)
    return out
```

```python
from contextlib import ExitStack

import numpy as np

import concourse.bass as bass
from concourse import mybir

F32 = mybir.dt.float32
BF16 = mybir.dt.bfloat16
I32 = mybir.dt.int32
ALU = mybir.AluOpType
ACT = mybir.ActivationFunctionType
AX = mybir.AxisListType.X
ENG = mybir.EngineType

P = 128
D = 64
HEADS = 4
HD = D // HEADS
K = 5
SLOTS = 5
SPLIT = 3
ROW = SPLIT * D
GROW = 200
CH = 7
EPS = 1e-5


def program(nc, x, edges, dst, W1l, b1, W1r, W2l, b2, W2r, Wq, bq, Wk, bk, We, be, Wv, bv, edge_attr, out):
    N = x.shape[0]
    E = dst.shape[0]
    NB = -(-N // P)
    FULL = N // P
    REST = N - FULL * P
    GE = P * K
    G = E // GE
    TURNS = G // SLOTS
    CHUNKS = NB // CH
    assert G * GE == E and TURNS * SLOTS == G and CHUNKS * CH == NB and TURNS <= P and REST > 0
    assert NB <= P

    x_rows = nc.dram_tensor("x_rows", (NB * P, ROW), BF16, kind="Internal").ap()
    h_rows = nc.dram_tensor("h_rows", (NB * P, ROW), BF16, kind="Internal").ap()
    kv_rows = nc.dram_tensor("kv_rows", (NB * P, 2 * D), F32, kind="Internal").ap()
    span_dram = nc.dram_tensor("span_dram", (2, TURNS, SLOTS), F32, kind="Internal").ap()

    with ExitStack() as ctx:
        def sb(name, shape, dt):
            return ctx.enter_context(nc.sbuf_tensor(name, shape, dt))

        def psum(name, shape, dt=F32):
            return ctx.enter_context(nc.psum_tensor(name, shape, dt))

        def sem(name):
            return ctx.enter_context(nc.semaphore(name))

        node_x = sb("node_x", [P, NB, 2 * D], F32)
        node_h = sb("node_h", [P, NB, 2 * D], F32)
        node_q = sb("node_q", [P, NB, ROW], BF16)
        degree = sb("degree", [P, NB], F32)

        edge_ids = sb("edge_ids", [P, SLOTS, 2 * K], I32)
        rows = sb("rows", [P, SLOTS, K, GROW], BF16)
        kv = sb("kv", [P, SLOTS, K, 2 * D], F32)
        attr = sb("attr", [P, SLOTS, K * D], F32)

        dst_local = sb("dst_local", [P, K], F32)
        hot = sb("hot", [P, K, P], BF16)
        hot32 = sb("hot32", [P, K, P], F32)
        hotT = sb("hotT", [P, K, P], BF16)
        part_sum = sb("part_sum", [P, D], F32)
        attrT = sb("attrT", [D + 1, K, P], F32)
        q_block = sb("q_block", [P, ROW], BF16)
        kq = sb("kq", [P, K, D], F32)
        kqe = sb("kqe", [P, K, D], F32)
        score = sb("score", [P, K * HEADS], F32)
        clipped = sb("clipped", [P, K * HEADS], F32)
        weight = sb("weight", [P, K * HEADS], F32)
        message = sb("message", [P, K, D], F32)

        stage = sb("stage", [P, CH, 2 * D], F32)
        stageT = sb("stageT", [P, CH, P], F32)
        mid = sb("mid", [P, CH, D], F32)
        mid2 = sb("mid2", [P, CH, D], F32)
        stat = sb("stat", [P, 6, CH], F32)
        split = sb("split", [P, CH, ROW], BF16)
        kv_out = sb("kv_out", [P, CH, 2 * D], F32)

        ident = sb("ident", [P, P], F32)
        ident16 = sb("ident16", [P, P], BF16)
        iota = sb("iota", [P, P], F32)
        base = sb("base", [P, NB], F32)
        w_in = sb("w_in", [D, 10, D], F32)
        w1 = sb("w1", [P, D], F32)
        w2 = sb("w2", [P, D], F32)
        wkvq = sb("wkvq", [D + 1, 3 * D], F32)
        we = sb("we", [D + 1, D], F32)
        bias = sb("bias", [P, 2, D], F32)

        span = sb("span", [TURNS, 2, SLOTS], F32)
        dst_all = node_q[0:TURNS].rearrange("p b f -> p (b f)").bitcast(I32)[:, 0:SLOTS * GE].rearrange(
            "p (r e) -> p r e", r=SLOTS)
        later = node_h[0:1].rearrange("p b f -> p (b f)")
        srow = later[:, 0:8 * G].rearrange("p (m g) -> p m g", m=8)
        irow = later[:, 8 * G:16 * G].bitcast(I32).rearrange("p (m g) -> p m g", m=8)
        table = sb("table", [1, TURNS, 8], I32)

        ps_sum = psum("ps_sum", [P, 512])
        ps_t = psum("ps_t", [P, 1024])
        ps_e = psum("ps_e", [P, 512])
        ps_hot = psum("ps_hot", [P, 1024], BF16)
        ps_q = psum("ps_q", [P, 512])
        ps_kv = psum("ps_kv", [P, 1024])

        x_in = sem("x_in")
        w_landed = sem("w_landed")
        dst_landed = sem("dst_landed")
        consts = sem("consts")
        wT = sem("wT")
        w_ready = sem("w_ready")
        setup = sem("setup")
        span_ready = sem("span_ready")
        span_stored = sem("span_stored")
        span_landed = sem("span_landed")
        table_ready = sem("table_ready")
        idents = sem("idents")
        stored = sem("stored")

        block = ctx.enter_context(nc.Block())

        def hold(engine):
            engine.nop(nofuse=True)

        class Pass:
            def __init__(self, name):
                self.ids = [sem(f"{name}_ids{u}") for u in range(SLOTS)]
                self.got = [sem(f"{name}_got{u}") for u in range(SLOTS)]
                self.attr = [sem(f"{name}_attr{u}") for u in range(SLOTS)] if name == "att" else None
                self.group_done = sem(f"{name}_group_done")
                self.hot = sem(f"{name}_hot")
                self.summed = sem(f"{name}_summed")
                self.added = sem(f"{name}_added")
                self.step = sem(f"{name}_step")
                if name == "att":
                    self.attr_t = sem("att_attr_t")
                    self.attr_c = sem("att_attr_c")
                    self.edge = sem("att_edge")
                    self.hot_t = sem("att_hot_t")
                    self.hot_c = sem("att_hot_c")
                    self.query = sem("att_query")
                    self.clipped = sem("att_clipped")
                    self.weight = sem("att_weight")
                    self.message = sem("att_message")

        class Dense:
            def __init__(self, name):
                self.staged = sem(f"{name}_staged")
                self.turned = sem(f"{name}_turned")
                self.copied = sem(f"{name}_copied")
                self.product = sem(f"{name}_product")
                self.step = sem(f"{name}_step")
                self.ready = sem(f"{name}_ready")
                self.rooted = sem(f"{name}_rooted")
                self.stored = sem(f"{name}_stored")

        sum_x, sum_h, att = Pass("sx"), Pass("sh"), Pass("att")
        d_split, d_one, d_two, d_kvq, d_end = (Dense(n) for n in ("split", "one", "two", "kvq", "end"))

        edges_v = edges.rearrange("g p c -> p g c")
        attr_v = edge_attr.rearrange("(g p k) d -> p g (k d)", p=P, k=K)
        x_rows_v = x_rows.rearrange("(b p) f -> p b f", p=P)
        h_rows_v = h_rows.rearrange("(b p) f -> p b f", p=P)
        kv_rows_v = kv_rows.rearrange("(b p) f -> p b f", p=P)
        x_full = x[0:FULL * P, :].rearrange("(b p) f -> p b f", p=P)
        out_full = out[0:FULL * P, :].rearrange("(b p) f -> p b f", p=P)

        def group_table(engine, turn):
            _, words = nc.values_load_multi_w_load_instructions(
                table[0:1, bass.ds(turn, 1), 0:SLOTS].rearrange("o a b -> o (a b)"),
                engines=[engine], min_val=0, max_val=2**31 - 1)
            return [(w >> 14, (w >> 7) & 127, w & 127) for w in words]

        def block_at(b):
            return nc.s_assert_within(b, 0, NB - 1)

        @block.sync
        def _(sp):
            sp.dma_start(dst_all, dst.rearrange("(q r e) -> q r e", q=TURNS, r=SLOTS)).then_inc(dst_landed, 16)
            for i, w in enumerate((W1l, W1r, W2l, W2r, Wk, Wv, Wq, We, We)):
                sp.dma_start(w_in[:, i, :], w).then_inc(w_landed, 16)
            for i, b in enumerate((bk, bv, bq)):
                sp.dma_start(wkvq[D:D + 1, i * D:(i + 1) * D], b.rearrange("(o d) -> o d", o=1)).then_inc(w_landed, 16)
            sp.dma_start(we[D:D + 1, :], be.rearrange("(o d) -> o d", o=1)).then_inc(w_landed, 16)
            for i, b in enumerate((b1, b2)):
                sp.dma_start(bias[:, i, :], b.rearrange("(o d) -> o d", o=1).to_broadcast([P, D])).then_inc(w_landed, 16)
            sp.dma_start(node_x[:, 0:FULL, D:2 * D], x_full).then_inc(x_in, 16)
            sp.wait_ge(consts, 1)
            sp.dma_start(node_x[0:REST, FULL, D:2 * D], x[FULL * P:N, :]).then_inc(x_in, 16)
            sp.wait_ge(span_ready, 1)
            sp.dma_start(span_dram.rearrange("m q r -> q m r"), span[:]).then_inc(span_stored, 16)
            sp.wait_ge(span_stored, 16)
            sp.dma_start(srow[:, 0:2, :], span_dram.rearrange("m q r -> m (q r)").rearrange("(o m) g -> o m g", o=1)).then_inc(span_landed, 16)

            def store_rows(d, view, tile):
                with sp.Fori(0, CHUNKS) as c:
                    sp.wait_ge(d.ready, c + 1)
                    sp.dma_start(view[:, bass.ds(c * CH, CH), :], tile).then_inc(d.stored, 16)

            def load_edges(p):
                with sp.Fori(0, TURNS) as t:
                    for u in range(SLOTS):
                        sp.wait_ge(p.group_done, t * SLOTS + u + 1)
                        sp.dma_start(edge_ids[:, u, :], edges_v[:, bass.ds(t * SLOTS + u, 1), :].rearrange("p a c -> p (a c)")).then_inc(p.ids[u], 16)
                        if p.attr:
                            sp.dma_start(attr[:, u, :], attr_v[:, bass.ds(t * SLOTS + u, 1), :].rearrange("p a c -> p (a c)")).then_inc(p.attr[u], 16)

            store_rows(d_split, x_rows_v, split[:])
            load_edges(sum_x)
            store_rows(d_one, h_rows_v, split[:])
            load_edges(sum_h)
            store_rows(d_kvq, kv_rows_v, kv_out[:])
            load_edges(att)
            sp.wait_ge(d_end.staged, 1)
            sp.dma_start(out_full, node_h[:, 0:FULL, D:2 * D]).then_inc(stored, 16)
            sp.dma_start(out[FULL * P:N, :], node_h[0:REST, FULL, D:2 * D]).then_inc(stored, 16)
            sp.wait_ge(stored, 32)

        @block.gpsimd
        def _(pool):
            nc.gpsimd.memset(ident[:], 0.0).then_inc(idents, 1)
            pool.wait_ge(idents, 1)
            nc.gpsimd.affine_select(out=ident[:], in_=ident[:], compare_op=ALU.not_equal, fill=1.0, base=0,
                                    pattern=[[-1, P]], channel_multiplier=1).then_inc(idents, 1)
            nc.gpsimd.iota(iota[:], pattern=[[1, P]], base=0, channel_multiplier=0,
                           allow_small_or_imprecise_dtypes=True).then_inc(idents, 1)
            nc.gpsimd.iota(base[:], pattern=[[P, NB]], base=0, channel_multiplier=0,
                           allow_small_or_imprecise_dtypes=True).then_inc(idents, 1)

            def gather(p, table_rows, into, width):
                with pool.Fori(0, TURNS) as t:
                    for u in range(SLOTS):
                        pool.wait_ge(p.ids[u], t * 16 + 16)
                        hold(pool)
                        for k in range(K):
                            nc.gpsimd.indirect_dma_start(
                                out=into[:, u, k, 0:width], out_offset=None, in_=table_rows,
                                in_offset=bass.IndirectOffsetOnAxis(ap=edge_ids[:, u, k:k + 1], axis=0),
                            ).then_inc(p.got[u], 16)

            pool.wait_ge(d_split.stored, 16 * CHUNKS)
            gather(sum_x, x_rows, rows, ROW)
            pool.wait_ge(d_one.stored, 16 * CHUNKS)
            gather(sum_h, h_rows, rows, ROW)
            pool.wait_ge(d_kvq.stored, 16 * CHUNKS)
            gather(att, kv_rows, kv, 2 * D)

        @block.tensor
        def _(pe):
            pe.wait_ge(idents, 2)
            pe.wait_ge(w_landed, 16 * 15)
            nc.tensor.transpose(ps_t[:, 0:D], w_in[:, 0:2, :].rearrange("p a b -> p (a b)"), ident[0:D, 0:D])
            nc.tensor.transpose(ps_t[:, D:2 * D], w_in[:, 2:4, :].rearrange("p a b -> p (a b)"), ident[0:D, 0:D])
            for i in range(4):
                last = nc.tensor.transpose(ps_t[0:D, 512 + i * D:512 + (i + 1) * D], w_in[:, 4 + i, :], ident[0:D, 0:D])
            last.then_inc(wT, 1)
            pe.wait_ge(w_ready, 1)

            def sum_pairs(p):
                with pe.Fori(0, TURNS) as t:
                    words = group_table(ENG.PE, t)
                    for u in range(SLOTS):
                        before, first, count = words[u]
                        pe.wait_ge(p.got[u], t * (16 * K) + 16 * K)
                        hold(pe)
                        with pe.Fori(0, count) as j:
                            pe.wait_ge(p.added, before + j + 1)
                            pe.wait_ge(p.hot, before + j + 1)
                            for k in range(K):
                                mm = nc.tensor.matmul(ps_sum[:, 0:ROW + 1], hot[:, k, :], rows[:, u, k, 0:ROW + 1],
                                                      start=(k == 0), stop=(k == K - 1))
                            mm.then_inc(p.summed, 1)

            def dense(d):
                with pe.Fori(0, CHUNKS) as c:
                    pe.wait_ge(d.staged, c + 1)
                    pe.wait_ge(d.rooted, c + 1)
                    for i in range(CH):
                        tp = nc.tensor.transpose(ps_t[:, i * P:(i + 1) * P], stage[:, i, :], ident[:])
                    tp.then_inc(d.turned, 1)
                    pe.wait_ge(d.copied, c + 1)
                    w = w1 if d is d_one else w2
                    for i in range(CH):
                        mm = nc.tensor.matmul(ps_q[:, i * D:(i + 1) * D], stageT[:, i, :], w[:], start=True, stop=True)
                    mm.then_inc(d.product, 1)

            def dense_kvq(d):
                with pe.Fori(0, CHUNKS) as c:
                    pe.wait_ge(d.staged, c + 1)
                    hold(pe)
                    for i in range(CH):
                        tp = nc.tensor.transpose(ps_t[0:D, i * P:(i + 1) * P], stage[:, i, 0:D], ident[:])
                    tp.then_inc(d.turned, 1)
                    pe.wait_ge(d.copied, c + 1)
                    for i in range(CH):
                        nc.tensor.matmul(ps_kv[:, i * 2 * D:(i + 1) * 2 * D], stageT[0:D + 1, i, :], wkvq[:, 0:2 * D],
                                         start=True, stop=True)
                        mm = nc.tensor.matmul(ps_q[:, i * D:(i + 1) * D], stageT[0:D + 1, i, :], wkvq[:, 2 * D:],
                                              start=True, stop=True)
                    mm.then_inc(d.product, 1)

            def attend(p):
                with pe.Fori(0, TURNS) as t:
                    words = group_table(ENG.PE, t)
                    for u in range(SLOTS):
                        before, first, count = words[u]
                        pe.wait_ge(p.attr[u], t * 16 + 16)
                        hold(pe)
                        with pe.Fori(0, count) as j:
                            n = before + j
                            pe.wait_ge(p.added, n + 1)
                            hold(pe)
                            for k in range(K):
                                tp = nc.tensor.transpose(ps_t[0:D, k * P:(k + 1) * P], attr[:, u, k * D:(k + 1) * D], ident[:])
                            tp.then_inc(p.attr_t, 1)
                            pe.wait_ge(p.hot, n + 1)
                            for k in range(K):
                                tp = nc.tensor.transpose(ps_hot[:, k * P:(k + 1) * P], hot[:, k, :], ident16[:])
                            tp.then_inc(p.hot_t, 1)
                            pe.wait_ge(p.attr_c, n + 1)
                            for k in range(K):
                                mm = nc.tensor.matmul(ps_e[:, k * D:(k + 1) * D], attrT[:, k, :], we[:], start=True, stop=True)
                            mm.then_inc(p.edge, 1)
                            pe.wait_ge(p.hot_c, n + 1)
                            for k in range(K):
                                for s in range(SPLIT):
                                    mm = nc.tensor.matmul(ps_q[:, k * D:(k + 1) * D], hotT[:, k, :], q_block[:, s * D:(s + 1) * D],
                                                          start=(s == 0), stop=(s == SPLIT - 1))
                            mm.then_inc(p.query, 1)
                            pe.wait_ge(p.message, n + 1)
                            for k in range(K):
                                mm = nc.tensor.matmul(ps_sum[:, 0:D], hot32[:, k, :], message[:, k, :],
                                                      start=(k == 0), stop=(k == K - 1))
                            mm.then_inc(p.summed, 1)

            pe.wait_ge(table_ready, 1)
            sum_pairs(sum_x)
            dense(d_one)
            sum_pairs(sum_h)
            dense(d_two)
            dense_kvq(d_kvq)
            attend(att)

        @block.scalar
        def _(act):
            act.wait_ge(table_ready, 1)

            def dense(d, roots):
                with act.Fori(0, CHUNKS) as c:
                    act.wait_ge(d.staged, c + 1)
                    nc.scalar.copy(stage[:, :, D:2 * D], roots[:, bass.ds(c * CH, CH), D:2 * D]).then_inc(d.rooted, 1)
                    act.wait_ge(d.turned, c + 1)
                    nc.scalar.copy(stageT[:], ps_t[:, 0:CH * P].rearrange("p (i j) -> p i j", i=CH)).then_inc(d.copied, 1)
                    if d is d_two:
                        act.wait_ge(d_two.ready, c + 1)
                        nc.scalar.activation(stat[:, 4, :], stat[:, 3, :], ACT.Sqrt).then_inc(d_two.stored, 1)

            dense(d_one, node_x)
            dense(d_two, node_h)
            with act.Fori(0, CHUNKS) as c:
                act.wait_ge(d_kvq.turned, c + 1)
                nc.scalar.copy(stageT[0:D, :, :], ps_t[0:D, 0:CH * P].rearrange("p (i j) -> p i j", i=CH)).then_inc(d_kvq.copied, 1)
            p = att
            with act.Fori(0, TURNS) as t:
                words = group_table(ENG.Activation, t)
                for u in range(SLOTS):
                    before, first, count = words[u]
                    with act.Fori(0, count) as j:
                        n = before + j
                        b = block_at(first + j)
                        act.wait_ge(p.attr_t, n + 1)
                        nc.scalar.copy(attrT[0:D, :, :], ps_t[0:D, 0:K * P].rearrange("p (i j) -> p i j", i=K)).then_inc(p.attr_c, 1)
                        nc.scalar.copy(q_block[:].rearrange("p (a f) -> p a f", a=1), node_q[:, bass.ds(b, 1), :])
                        act.wait_ge(p.hot_t, n + 1)
                        nc.scalar.copy(hotT[:], ps_hot[:, 0:K * P].rearrange("p (i j) -> p i j", i=K)).then_inc(p.hot_c, 1)
                        act.wait_ge(p.clipped, n + 1)
                        nc.scalar.activation(weight[:], clipped[:], ACT.Exp).then_inc(p.weight, 1)
            with act.Fori(0, CHUNKS) as c:
                act.wait_ge(d_end.ready, c + 1)
                nc.scalar.activation(stat[:, 4, :], stat[:, 3, :], ACT.Sqrt).then_inc(d_end.stored, 1)

        @block.vector
        def _(dve):
            v = nc.vector

            class Steps:
                def __init__(self, s, base=0):
                    self.s, self.base, self.n = s, base, 0

                def link(self, ins):
                    ins.then_inc(self.s, 1)
                    self.n += 1
                    dve.wait_ge(self.s, self.base + self.n)

            st = Steps(setup)
            v.memset(node_x[:, FULL, :], 0.0).then_inc(consts, 1)
            v.memset(node_x[:, 0:FULL, 0:D], 0.0)
            v.memset(degree[:], 0.0)
            v.memset(rows[:, :, :, ROW:GROW], 1.0)
            v.memset(attrT[D:D + 1, :, :], 1.0)
            st.link(v.memset(table[:], 0))
            dve.wait_ge(dst_landed, 16)
            v.tensor_reduce(span[:, 0, :], dst_all, AX, ALU.min)
            v.tensor_reduce(span[:, 1, :], dst_all, AX, ALU.max).then_inc(span_ready, 1)
            dve.wait_ge(idents, 4)
            v.tensor_copy(ident16[:], ident[:])
            dve.wait_ge(wT, 1)
            v.tensor_copy(w1[:], ps_t[:, 0:D])
            v.tensor_copy(w2[:], ps_t[:, D:2 * D])
            v.tensor_copy(wkvq[0:D, :], ps_t[0:D, 512:512 + 3 * D])
            st.link(v.tensor_copy(we[0:D, :], ps_t[0:D, 512 + 3 * D:512 + 4 * D]))
            v.memset(stat[:], 0.0).then_inc(w_ready, 1)
            dve.wait_ge(span_landed, 16)
            st.link(v.tensor_copy(irow[:, 0:2, :], srow[:, 0:2, :]))
            st.link(v.tensor_single_scalar(irow[:, 2:4, :], irow[:, 0:2, :], 7, ALU.arith_shift_right))
            st.link(v.tensor_copy(srow[:, 2:4, :], irow[:, 2:4, :]))
            st.link(v.tensor_tensor(srow[:, 4, :], srow[:, 3, :], srow[:, 2, :], ALU.subtract))
            st.link(v.tensor_scalar_add(srow[:, 4, :], srow[:, 4, :], 1.0))
            st.link(v.memset(srow[:, 5, :], 1.0))
            st.link(v.tensor_tensor_scan(srow[:, 6, :], srow[:, 5, :], srow[:, 4, :], 0.0, ALU.mult, ALU.add))
            st.link(v.tensor_tensor(srow[:, 7, :], srow[:, 6, :], srow[:, 4, :], ALU.subtract))
            st.link(v.tensor_copy(irow[:, 4, :], srow[:, 4, :]))
            st.link(v.tensor_copy(irow[:, 5, :], srow[:, 7, :]))
            st.link(v.tensor_single_scalar(irow[:, 6, :], irow[:, 5, :], 14, ALU.logical_shift_left))
            st.link(v.tensor_single_scalar(irow[:, 7, :], irow[:, 2, :], 7, ALU.logical_shift_left))
            st.link(v.tensor_tensor(irow[:, 6, :], irow[:, 6, :], irow[:, 7, :], ALU.bitwise_or))
            v.tensor_tensor(table[:, :, 0:SLOTS], irow[:, 6, :].rearrange("o (q r) -> o q r", r=SLOTS),
                            irow[:, 4, :].rearrange("o (q r) -> o q r", r=SLOTS), ALU.bitwise_or).then_inc(table_ready, 1)
            dve.wait_ge(table_ready, 1)
            v.memset(node_h[:], 0.0)

            for p in (sum_x, sum_h, att):
                v.engine_nop().then_inc(p.added, 1)
                for _ in range(SLOTS):
                    v.engine_nop().then_inc(p.group_done, 1)

            def split_rows(s, src, split, ready):
                s.link(v.tensor_scalar_mul(split[:, :, 0:D], src, 1.0))
                s.link(v.tensor_tensor(mid[:], src, split[:, :, 0:D], ALU.subtract))
                s.link(v.tensor_scalar_mul(split[:, :, D:2 * D], mid[:], 1.0))
                v.tensor_tensor(split[:, :, 2 * D:], mid[:], split[:, :, D:2 * D], ALU.subtract).then_inc(ready, 1)

            def one_hot(p, u, b, s):
                s.link(v.tensor_scalar(dst_local[:], edge_ids[:, u, K:2 * K], base[:, bass.ds(b, 1)], None, ALU.subtract))
                o = hot32 if p is att else hot
                ins = v.tensor_tensor(o[:], dst_local[:].rearrange("p (k o) -> p k o", o=1).to_broadcast([P, K, P]),
                                      iota[:].rearrange("p (o n) -> p o n", o=1).to_broadcast([P, K, P]), ALU.is_equal)
                if p is att:
                    s.link(ins)
                    ins = v.tensor_copy(hot[:], hot32[:])
                ins.then_inc(p.hot, 1)

            def sum_pairs(p, nodes, count_edges):
                STEPS = 2
                with dve.Fori(0, TURNS) as t:
                    words = group_table(ENG.DVE, t)
                    for u in range(SLOTS):
                        before, first, count = words[u]
                        dve.wait_ge(p.ids[u], t * 16 + 16)
                        hold(dve)
                        with dve.Fori(0, count) as j:
                            n = before + j
                            b = block_at(first + j)
                            s = Steps(p.step, n * STEPS)
                            one_hot(p, u, b, s)
                            dve.wait_ge(p.added, n + 1)
                            dve.wait_ge(p.summed, n + 1)
                            s.link(v.tensor_reduce(part_sum[:], ps_sum[:, 0:ROW].rearrange("p (s f) -> p f s", s=SPLIT), AX, ALU.add))
                            if count_edges:
                                v.tensor_tensor(degree[:, bass.ds(b, 1)], degree[:, bass.ds(b, 1)], ps_sum[:, ROW:ROW + 1], ALU.add)
                            v.tensor_tensor(nodes[:, bass.ds(b, 1), 0:D], nodes[:, bass.ds(b, 1), 0:D],
                                            part_sum[:].rearrange("p (o f) -> p o f", o=1), ALU.add).then_inc(p.added, 1)
                        v.engine_nop().then_inc(p.group_done, 1)

            def mean_rows(d, s, c, nodes):
                v.tensor_tensor(stage[:, :, 0:D], nodes[:, bass.ds(c * CH, CH), 0:D],
                                       degree[:, bass.ds(c * CH, CH)].rearrange("p (i o) -> p i o", o=1).to_broadcast([P, CH, D]), ALU.mult).then_inc(d.staged, 1)
                dve.wait_ge(d.product, c + 1)

            def layer_norm(d, s, z, z_out, c):
                wide = lambda a: a.rearrange("p (i o) -> p i o", o=1).to_broadcast([P, CH, D])
                s.link(v.tensor_reduce(stat[:, 0, :], z, AX, ALU.add))
                s.link(v.tensor_scalar_mul(stat[:, 1, :], stat[:, 0, :], 1.0 / D))
                s.link(v.tensor_tensor(mid[:], z, wide(stat[:, 1, :]), ALU.subtract))
                s.link(v.tensor_tensor(mid2[:], mid[:], mid[:], ALU.mult))
                s.link(v.tensor_reduce(stat[:, 2, :], mid2[:], AX, ALU.add))
                v.tensor_scalar(stat[:, 3, :], stat[:, 2, :], 1.0 / D, EPS, ALU.mult, ALU.add).then_inc(d.ready, 1)
                dve.wait_ge(d.stored, c + 1)
                s.link(v.reciprocal(stat[:, 5, :], stat[:, 4, :]))
                s.link(v.tensor_tensor(z_out, mid[:], wide(stat[:, 5, :]), ALU.mult))

            dve.wait_ge(x_in, 32)
            with dve.Fori(0, CHUNKS) as c:
                s = Steps(d_split.step, c * 3)
                split_rows(s, node_x[:, bass.ds(c * CH, CH), D:2 * D], split[:], d_split.ready)
                dve.wait_ge(d_split.stored, c * 16 + 16)
                hold(dve)

            sum_pairs(sum_x, node_x, True)
            dve.wait_ge(sum_x.group_done, SLOTS + G)
            st.link(v.tensor_scalar_max(degree[:], degree[:], 1.0))
            st.link(v.reciprocal(degree[:], degree[:]))

            with dve.Fori(0, CHUNKS) as c:
                s = Steps(d_one.step, c * 5)
                mean_rows(d_one, s, c, node_x)
                s.link(v.tensor_tensor(mid2[:], ps_q[:, 0:CH * D].rearrange("p (i f) -> p i f", i=CH),
                                       bias[:, 0:1, :].to_broadcast([P, CH, D]), ALU.add))
                h = node_h[:, bass.ds(c * CH, CH), D:2 * D]
                s.link(v.tensor_scalar_max(h, mid2[:], 0.0))
                split_rows(s, h, split[:], d_one.ready)
                dve.wait_ge(d_one.stored, c * 16 + 16)
                hold(dve)

            sum_pairs(sum_h, node_h, False)
            dve.wait_ge(sum_h.group_done, SLOTS + G)

            with dve.Fori(0, CHUNKS) as c:
                s = Steps(d_two.step, c * 9)
                mean_rows(d_two, s, c, node_h)
                s.link(v.tensor_tensor(mid2[:], ps_q[:, 0:CH * D].rearrange("p (i f) -> p i f", i=CH),
                                       bias[:, 1:2, :].to_broadcast([P, CH, D]), ALU.add))
                xs = node_x[:, bass.ds(c * CH, CH), D:2 * D]
                s.link(v.tensor_tensor(mid[:], mid2[:], xs, ALU.add))
                layer_norm(d_two, s, mid[:], xs, c)

            st.link(v.memset(stageT[D:D + 1, :, :], 1.0))
            with dve.Fori(0, CHUNKS) as c:
                s = Steps(d_kvq.step, c * 5)
                v.tensor_copy(stage[:, :, 0:D], node_x[:, bass.ds(c * CH, CH), D:2 * D]).then_inc(d_kvq.staged, 1)
                dve.wait_ge(d_kvq.product, c + 1)
                s.link(v.tensor_scalar_mul(mid2[:], ps_q[:, 0:CH * D].rearrange("p (i f) -> p i f", i=CH), HD ** -0.5))
                v.tensor_copy(kv_out[:], ps_kv[:, 0:CH * 2 * D].rearrange("p (i f) -> p i f", i=CH)).then_inc(d_kvq.ready, 1)
                split_rows(s, mid2[:], node_q[:, bass.ds(c * CH, CH), :], d_kvq.step)
                dve.wait_ge(d_kvq.step, c * 5 + 5)
                dve.wait_ge(d_kvq.stored, c * 16 + 16)
                hold(dve)

            st.link(v.memset(node_x[:, :, 0:D], 0.0))
            p = att
            STEPS = 5
            with dve.Fori(0, TURNS) as t:
                words = group_table(ENG.DVE, t)
                for u in range(SLOTS):
                    before, first, count = words[u]
                    dve.wait_ge(p.ids[u], t * 16 + 16)
                    dve.wait_ge(p.got[u], t * (16 * K) + 16 * K)
                    hold(dve)
                    with dve.Fori(0, count) as j:
                        n = before + j
                        b = block_at(first + j)
                        s = Steps(p.step, n * STEPS)
                        one_hot(p, u, b, s)
                        dve.wait_ge(p.query, n + 1)
                        s.link(v.tensor_tensor(kq[:], kv[:, u, :, 0:D], ps_q[:, 0:K * D].rearrange("p (k f) -> p k f", k=K), ALU.mult))
                        dve.wait_ge(p.edge, n + 1)
                        s.link(v.tensor_tensor(kqe[:], kq[:], ps_e[:, 0:K * D].rearrange("p (k f) -> p k f", k=K), ALU.mult))
                        s.link(v.tensor_reduce(score[:], kqe[:].rearrange("p k (h f) -> p (k h) f", h=HEADS), AX, ALU.add))
                        v.tensor_scalar(clipped[:], score[:], -5.0, 5.0, ALU.max, ALU.min).then_inc(p.clipped, 1)
                        dve.wait_ge(p.weight, n + 1)
                        v.tensor_tensor(
                            message[:].rearrange("p k (h f) -> p k h f", h=HEADS),
                            kv[:, u, :, D:2 * D].rearrange("p k (h f) -> p k h f", h=HEADS),
                            weight[:].rearrange("p (k h o) -> p k h o", k=K, o=1).to_broadcast([P, K, HEADS, HD]), ALU.mult).then_inc(p.message, 1)
                        dve.wait_ge(p.added, n + 1)
                        dve.wait_ge(p.summed, n + 1)
                        v.tensor_tensor(node_x[:, bass.ds(b, 1), 0:D], node_x[:, bass.ds(b, 1), 0:D],
                                        ps_sum[:, 0:D].rearrange("p (o f) -> p o f", o=1), ALU.add).then_inc(p.added, 1)
                    v.engine_nop().then_inc(p.group_done, 1)

            dve.wait_ge(att.group_done, SLOTS + G)
            with dve.Fori(0, CHUNKS) as c:
                s = Steps(d_end.step, c * 8)
                s.link(v.tensor_tensor(mid[:], node_x[:, bass.ds(c * CH, CH), 0:D], node_x[:, bass.ds(c * CH, CH), D:2 * D], ALU.add))
                layer_norm(d_end, s, mid[:], node_h[:, bass.ds(c * CH, CH), D:2 * D], c)
            v.engine_nop().then_inc(d_end.staged, 1)


def kernel(**inputs):
    import concourse.bacc as bacc
    from concourse.bass_utils import run_bass_kernel_spmd as run

    E = inputs["src"].shape[0]
    ids = [np.asarray(inputs[n]).reshape(E // (P * K), P, K) for n in ("src", "dst")]
    arrays = {"x": inputs["x"], "edges": np.concatenate(ids, axis=2), "dst": inputs["dst"]}
    for n in ("L0_gnn_W1_l", "L0_gnn_b1_l", "L0_gnn_W1_r", "L0_gnn_W2_l", "L0_gnn_b2_l", "L0_gnn_W2_r",
              "L1_gnn_Wq", "L1_gnn_bq", "L1_gnn_Wk", "L1_gnn_bk", "L1_gnn_We", "L1_gnn_be", "L1_gnn_Wv", "L1_gnn_bv",
              "edge_attr_64"):
        arrays[n] = inputs[n]
    nc = bacc.Bacc("TRN2", target_bir_lowering=False, num_devices=1)
    feeds, args = {}, []
    for n, a in arrays.items():
        a = np.ascontiguousarray(a)
        feeds[f"in_{n}"] = a
        args.append(nc.dram_tensor(f"in_{n}", a.shape, mybir.dt.from_np(a.dtype), kind="ExternalInput").ap())
    shape = tuple(np.asarray(inputs["x"]).shape)
    args.append(nc.dram_tensor("out_0", shape, F32, kind="ExternalOutput").ap())
    program(nc, *args)
    r = run(nc, [feeds], core_ids=[0])
    return r.results[0]["out_0"]
```
